# Optimizing a Trainium2 kernel written in Bass

```python
import numpy as np
import jax
import jax.numpy as jnp

def _softmax(x, axis=-1):
    return jax.nn.softmax(x, axis=axis)

def _gelu(x):
    return jax.nn.gelu(x, approximate=True)

def _silu(x):
    return jax.nn.silu(x)

def _sigmoid(x):
    return jax.nn.sigmoid(x)

def _layernorm(x, axis=-1, eps=1e-05):
    m = jnp.mean(x, axis=axis, keepdims=True)
    v = jnp.var(x, axis=axis, keepdims=True)
    return (x - m) / jnp.sqrt(v + eps)

def _scatter_add(tgt, idx, src, axis=0):
    return tgt.at[idx].add(src)

def _segment_sum(src, seg, n):
    return jax.ops.segment_sum(src, seg, n)
kernel_name = 'mk_adj_resnorm_d2_adj_r2_d65467'

def setup_inputs(seed: int=0):
    np.random.seed(seed)
    _w = jnp.asarray

    def _rec_inputs():
        import jax
        import jax.numpy as jnp
        _gk = jax.random.key(seed)
        x = -0.000929 + 1 * jax.random.normal(jax.random.fold_in(_gk, 1), (8192, 64), jnp.float32)
        _a = jax.random.bernoulli(jax.random.fold_in(_gk, 2), 0.000976562, (8192, 8192))
        _a = jnp.logical_or(_a, jnp.swapaxes(_a, -1, -2))
        _a = jnp.logical_or(_a, jnp.eye(8192, dtype=bool))
        _af = _a.astype(jnp.float32)
        _af = _af * jax.random.uniform(jax.random.fold_in(_gk, 3), (8192, 8192), jnp.float32, 0.05, 1)
        adj = _af
        return (x, adj)
    x, adj = _rec_inputs()

    def _L0_gnn_setup():
        import jax, jax.numpy as jnp
        import numpy as np
        N = 8192
        IN_C = 64
        OUT_C = 64
        key = jax.random.key(seed)
        k1, k2, k3 = jax.random.split(key, 3)
        x = jax.random.normal(k1, (N, IN_C), dtype=jnp.float32)
        adj = jax.random.uniform(k2, (N, N), dtype=jnp.float32)
        scale = jnp.sqrt(6.0 / (IN_C + OUT_C))
        weight = jax.random.uniform(k3, (IN_C, OUT_C), dtype=jnp.float32, minval=-scale, maxval=scale)
        return {'x': x, 'adj': adj, 'weight': weight}
    _L0_gnn_all = _L0_gnn_setup()
    _L0_gnn_in = {k: v for k, v in _L0_gnn_all.items() if k in ('weight',)}
    del _L0_gnn_all

    def _L1_gnn_setup():
        import jax, jax.numpy as jnp
        import numpy as np
        N = 8192
        IN_C = 64
        OUT_C = 64
        key = jax.random.key(seed)
        k1, k2, k3 = jax.random.split(key, 3)
        g_data = jax.random.normal(k1, (N, IN_C), dtype=jnp.float32)
        g_adj = jax.random.uniform(k2, (N, N), dtype=jnp.float32)
        bound = 1.44 * np.sqrt(6.0 / (IN_C + OUT_C))
        W = jax.random.uniform(k3, (IN_C, OUT_C), dtype=jnp.float32, minval=-bound, maxval=bound)
        return {'g_data': g_data, 'g_adj': g_adj, 'W': W}
    _L1_gnn_all = _L1_gnn_setup()
    _L1_gnn_in = {k: v for k, v in _L1_gnn_all.items() if k in ('W',)}
    del _L1_gnn_all
    return {'x': x, 'adj': adj, 'L0_gnn_weight': _L0_gnn_in['weight'], 'L1_gnn_W': _L1_gnn_in['W']}

def reference(x, adj, L0_gnn_weight, L1_gnn_W):
    import jax
    import jax.numpy as jnp

    def _L0_gnn_ref(x, adj, weight):
        import jax, jax.numpy as jnp
        import numpy as np
        N = 8192
        IN_C = 64
        OUT_C = 64
        agg = adj @ x
        return agg @ weight

    def _L1_gnn_ref(g_data, g_adj, W):
        import jax, jax.numpy as jnp
        import numpy as np
        N = 8192
        IN_C = 64
        OUT_C = 64
        n = g_adj.shape[0]
        a = g_adj + jnp.eye(n, dtype=g_adj.dtype)
        deg = a.sum(axis=1)
        dinv = jnp.where(deg > 0, deg ** (-0.5), 0.0)
        a_norm = dinv[:, None] * a * dinv[None, :]
        out = a_norm @ g_data
        out = out @ W
        return out
    x = _layernorm(x + _L0_gnn_ref(x, adj, L0_gnn_weight), axis=-1)
    x = _layernorm(x + _L1_gnn_ref(x, adj, L1_gnn_W), axis=-1)
    return x

_drawn_inputs = setup_inputs


def setup_inputs(seed=0):
    import zlib

    import numpy as np

    out = dict(_drawn_inputs(seed))
    spreads = {}
    factors = {}
    for name, (base, spread) in spreads.items():
        noise = np.random.default_rng([zlib.crc32(name.encode()), seed]).standard_normal(out[name].shape)
        drawn = base * np.exp(spread * noise) if base else spread * noise
        out[name] = jnp.asarray(drawn.astype(out[name].dtype))
    for name, factor in factors.items():
        out[name] = (out[name] * factor).astype(out[name].dtype)
    return out
```

```python
from contextlib import ExitStack

import concourse.bass as bass
from concourse import mybir

F32 = mybir.dt.float32
ALU = mybir.AluOpType
ACT = mybir.ActivationFunctionType
AX_X = mybir.AxisListType.X

P = 128
EPS = 1e-5
TINY = 1.1754944e-38
CHUNK_TILES = 2
RING = 16
COLS = 512
BLOCK = 2 * COLS
GROUP = 4


def two_layers(nc, adj_chunks, xT_halves, weights, consts, out):
    n_chunks = adj_chunks.shape[0]
    D = weights.shape[1] // 3
    N = 2 * xT_halves.shape[1]
    BLOCKS = N // BLOCK
    TILES = N // P
    BT = BLOCK // P
    HT = BT // 2
    CHUNKS = TILES // CHUNK_TILES
    HALVES = n_chunks // RING
    GROUPS = TILES // GROUP
    assert 2 * D == P and CHUNKS == 2 * RING and HALVES == 2 * BLOCKS

    with ExitStack() as ctx:
        def sb(name, shape):
            return ctx.enter_context(nc.sbuf_tensor(name, shape, F32))

        def psum(name, shape):
            return ctx.enter_context(nc.psum_tensor(name, shape, F32))

        def sem(name):
            return ctx.enter_context(nc.semaphore(name))

        ring = sb("ring", [P, RING, CHUNK_TILES, BLOCK])
        xT = sb("xT", [P, N // 2])
        w_sb = sb("w_sb", [P, 3 * D])
        c_sb = sb("c_sb", [P, 4 * D])
        w1c = sb("w1c", [P, D])
        from_x = sb("from_x", [P, 3 * D])
        from_agg = sb("from_agg", [P, 2 * D])
        y = sb("y", [P, TILES, D])
        g = sb("g", [P, TILES, D])
        z = sb("z", [P, TILES, D])
        dinv = sb("dinv", [P, TILES])
        agg_sb = sb("agg_sb", [P, COLS])
        mixed = sb("mixed", [P, BT, D])
        squares = sb("squares", [P, BT, D])
        out_sb = sb("out_sb", [P, BT, D])
        sums = sb("sums", [P, BT])
        stat = sb("stat", [P, 2 * BT])
        root = sb("root", [P, 2 * BT])
        rs = sb("rs", [P, 2 * BT])
        ra = sb("ra", [P, 2 * BT])
        rb = sb("rb", [P, 2 * BT])
        mask = sb("mask", [P, BT])
        gain = sb("gain", [P, BT])

        cent, ident = c_sb[:, 0:D], c_sb[:, D:2 * D]
        expand, expandT = c_sb[:, 2 * D:3 * D], c_sb[:, 3 * D:4 * D]
        w0T, w1T = w_sb[:, 0:D], w_sb[:, D:2 * D]

        agg = psum("agg", [P, COLS])
        tiles_ps = psum("tiles_ps", [P, BT, P])
        x_ps = psum("x_ps", [P, 2, GROUP, 4 * D])
        deg_ps = x_ps[:, :, 0, 0:HT]

        weights_loaded = sem("weights_loaded")
        x_loaded = sem("x_loaded")
        chunk_loaded = [sem(f"chunk_loaded{s}") for s in range(RING)]
        chunk_used = sem("chunk_used")
        folds_done = sem("folds_done")
        folds_copied = sem("folds_copied")
        consts_copied = sem("consts_copied")
        y_ones = sem("y_ones")
        x_products = sem("x_products")
        x_copied = [sem(f"x_copied_by_{e}") for e in ("scalar", "vector")]
        agg_copied = sem("agg_copied")
        tiles_done = sem("tiles_done")
        rows_mixed = sem("rows_mixed")
        squared = sem("squared")
        stat_ready = sem("stat_ready")
        rooted = sem("rooted")
        z_ready = sem("z_ready")
        out_ready = sem("out_ready")
        out_stored = sem("out_stored")
        dve_step = sem("dve_step")

        block = ctx.enter_context(nc.Block())

        @block.sync
        def _(sp):
            sp.dma_start(w_sb[:], weights).then_inc(weights_loaded, 16)
            sp.dma_start(c_sb[:], consts).then_inc(weights_loaded, 16)
            sp.dma_start(xT[:], xT_halves).then_inc(x_loaded, 16)
            for s in range(RING):
                sp.dma_start(ring[:, s], adj_chunks[s]).then_inc(chunk_loaded[s], 16)
            with sp.Fori(0, HALVES - 1) as m:
                for s in range(RING):
                    sp.wait_ge(chunk_used, RING * m + (s + 1))
                    sp.dma_start(ring[:, s], adj_chunks[bass.ds(RING * m + (RING + s), 1)].squeeze(0)
                                 ).then_inc(chunk_loaded[s], 16)
            with sp.Fori(0, HALVES - 1) as q:
                first = sp.snap(q * -RING + (HALVES - 2) * RING)
                for s in range(RING):
                    sp.wait_ge(chunk_used, RING * q + (RING * HALVES + s + 1))
                    sp.dma_start(ring[:, s],
                                 adj_chunks[bass.ds(first + s, 1)].squeeze(0)
                                 ).then_inc(chunk_loaded[s], 16)

        @block.tensor
        def _(pe):
            def add_chunk(stationary, half, s, first, last):
                for k in range(CHUNK_TILES):
                    t = (half * RING + s) * CHUNK_TILES + k
                    for a in range(2):
                        mm = pe.matmul(agg[D * a:D * a + D, :], stationary[:, t, :],
                                       ring[:, s, k, COLS * a:COLS * a + COLS],
                                       start=first and k == 0, stop=last and k == CHUNK_TILES - 1)
                return mm

            pe.wait_ge(weights_loaded, 32)
            for a in range(2):
                lo, hi = D * a, D * a + D
                pe.matmul(agg[lo:hi, 0:D], w0T[lo:hi], cent[lo:hi], start=True, stop=True)
                mm = pe.matmul(agg[lo:hi, D:2 * D], w1T[lo:hi], cent[lo:hi], start=True, stop=True)
            mm.then_inc(folds_done, 1)
            pe.wait_ge(folds_copied, 1)
            for a in range(2):
                lo, hi = D * a, D * a + D
                pe.matmul(agg[lo:hi, 2 * D:3 * D], cent[lo:hi], w1c[lo:hi], start=True, stop=True)
                mm = pe.matmul(agg[lo:hi, 3 * D:4 * D], expandT[lo:hi], w1c[lo:hi],
                               start=True, stop=True)
            mm.then_inc(folds_done, 1)

            pe.wait_ge(folds_copied, 2)
            pe.wait_ge(consts_copied, 1)
            pe.wait_ge(x_loaded, 16)
            for q in range(GROUPS):
                if q >= 2:
                    pe.wait_ge(x_copied[q % 2], q // 2)
                for k in range(GROUP):
                    a, col = divmod((q * GROUP + k) * P, N // 2)
                    mm = pe.matmul(x_ps[:, q % 2, k, 0:3 * D], xT[D * a:D * a + D, col:col + P],
                                   from_x[D * a:D * a + D, :], start=True, stop=True)
                mm.then_inc(x_products, 1)
            for reader in x_copied:
                pe.wait_ge(reader, GROUPS // 2)

            with pe.Fori(0, BLOCKS) as b:
                for c in range(CHUNKS):
                    half, s = divmod(c, RING)
                    pe.wait_ge(chunk_loaded[s], 32 * b + 16 * (half + 1))
                    add_chunk(y, half, s, c == 0, c == CHUNKS - 1).then_inc(chunk_used, 1)
                pe.wait_ge(agg_copied, b + 1)
                for t in range(BT):
                    a, q = divmod(t, HT)
                    part = agg_sb[D * a:D * a + D, q * P:(q + 1) * P]
                    pe.matmul(tiles_ps[:, t, :], part, from_agg[D * a:D * a + D, :],
                              start=True, stop=True)
                    mm = pe.matmul(deg_ps[:, a, q:q + 1], part, ident[D * a:D * a + D, D - 1:D],
                                   start=True, stop=True)
                mm.then_inc(tiles_done, 1)

            with pe.Fori(0, BLOCKS) as b:
                pe.wait_ge(z_ready, BLOCKS - 1)
                for c in range(CHUNKS):
                    half, s = 1 - c // RING, c % RING
                    if c * CHUNK_TILES == TILES // 2 - BT:
                        pe.wait_ge(z_ready, BLOCKS)
                    pe.wait_ge(chunk_loaded[s], 32 * b + 16 * (HALVES + c // RING))
                    add_chunk(z, half, s, c == 0, c == CHUNKS - 1).then_inc(chunk_used, 1)
                pe.wait_ge(agg_copied, b + (BLOCKS + 1))
                for t in range(BT):
                    a, q = divmod(t, HT)
                    mm = pe.matmul(tiles_ps[:, t, 0:D],
                                   agg_sb[D * a:D * a + D, q * P:(q + 1) * P],
                                   ident[D * a:D * a + D, :], start=True, stop=True)
                mm.then_inc(tiles_done, 1)

        @block.scalar
        def _(act):
            act.wait_ge(weights_loaded, 32)
            nc.scalar.copy(from_x[:, D:2 * D], cent)
            nc.scalar.copy(from_agg[:, 0:D], expand).then_inc(consts_copied, 1)

            for q in range(0, GROUPS, 2):
                act.wait_ge(x_products, q + 1)
                rows = slice(q * GROUP, (q + 1) * GROUP)
                nc.scalar.copy(y[:, rows, 0:D - 1], x_ps[:, 0, :, 0:D - 1])
                nc.scalar.copy(g[:, rows, :], x_ps[:, 0, :, D:2 * D])
                nc.scalar.copy(z[:, rows, :], x_ps[:, 0, :, 2 * D:3 * D]).then_inc(x_copied[0], 1)

            with act.Fori(0, BLOCKS) as b:
                act.wait_ge(chunk_used, CHUNKS * b + CHUNKS)
                nc.scalar.copy(agg_sb[:], agg[:]).then_inc(agg_copied, 1)
                act.wait_ge(rows_mixed, b + 1)
                nc.scalar.activation(squares[:], g[:, bass.ds(BT * b, BT), :], ACT.Square
                                     ).then_inc(squared, 1)
                act.wait_ge(stat_ready, b + 1)
                nc.scalar.activation(root[:], stat[:], ACT.Sqrt).then_inc(rooted, 1)

            with act.Fori(0, BLOCKS) as b:
                act.wait_ge(chunk_used, CHUNKS * b + CHUNKS * (BLOCKS + 1))
                nc.scalar.copy(agg_sb[:], agg[:]).then_inc(agg_copied, 1)
                act.wait_ge(rows_mixed, b + (BLOCKS + 1))
                nc.scalar.activation(squares[:], mixed[:], ACT.Square).then_inc(squared, 1)
                act.wait_ge(stat_ready, b + (BLOCKS + 1))
                nc.scalar.activation(root[:, 0:BT], stat[:, 0:BT], ACT.Sqrt).then_inc(rooted, 1)
                act.wait_ge(out_ready, b + 1)
                act.dma_start(out[bass.ds(b * -1 + (BLOCKS - 1), 1)].squeeze(0), out_sb[:]
                              ).then_inc(out_stored, 16)
                act.wait_ge(out_stored, 16 * b + 16)

        @block.vector
        def _(dve):
            v = nc.vector
            V1, V2 = 11, 8
            S2 = V1 * BLOCKS

            def inverse_root(n, at):
                v.reciprocal(rs[:, 0:n], root[:, 0:n]).then_inc(dve_step, 1)
                dve.wait_ge(dve_step, at + 1)
                v.tensor_tensor(ra[:, 0:n], stat[:, 0:n], rs[:, 0:n], ALU.mult).then_inc(dve_step, 1)
                dve.wait_ge(dve_step, at + 2)
                v.tensor_tensor(rb[:, 0:n], ra[:, 0:n], rs[:, 0:n], ALU.mult).then_inc(dve_step, 1)
                dve.wait_ge(dve_step, at + 3)
                v.tensor_scalar(ra[:, 0:n], rb[:, 0:n], -0.5, 1.5, ALU.mult, ALU.add
                                ).then_inc(dve_step, 1)
                dve.wait_ge(dve_step, at + 4)
                v.tensor_tensor(rb[:, 0:n], ra[:, 0:n], rs[:, 0:n], ALU.mult).then_inc(dve_step, 1)
                dve.wait_ge(dve_step, at + 5)

            def over_features(column):
                return column.unsqueeze(2).to_broadcast([P, BT, D])

            v.memset(y[:, :, D - 1:D], 1.0).then_inc(y_ones, 1)
            dve.wait_ge(folds_done, 1)
            v.tensor_copy(from_x[:, 0:D], agg[:, 0:D])
            v.tensor_copy(w1c[:], agg[:, D:2 * D]).then_inc(folds_copied, 1)
            dve.wait_ge(folds_done, 2)
            v.tensor_copy(from_x[:, 2 * D:3 * D], agg[:, 2 * D:3 * D])
            v.tensor_copy(from_agg[:, D:2 * D], agg[:, 3 * D:4 * D]).then_inc(folds_copied, 1)

            for q in range(1, GROUPS, 2):
                dve.wait_ge(x_products, q + 1)
                rows = slice(q * GROUP, (q + 1) * GROUP)
                v.tensor_copy(y[:, rows, 0:D - 1], x_ps[:, 1, :, 0:D - 1])
                v.tensor_copy(g[:, rows, :], x_ps[:, 1, :, D:2 * D])
                v.tensor_copy(z[:, rows, :], x_ps[:, 1, :, 2 * D:3 * D]).then_inc(x_copied[1], 1)
            for reader in x_copied:
                dve.wait_ge(reader, GROUPS // 2)

            with dve.Fori(0, BLOCKS) as b:
                gb = g[:, bass.ds(BT * b, BT), :]
                zb = z[:, bass.ds(BT * b, BT), :]
                deg = stat[:, BT:2 * BT]
                dve.wait_ge(tiles_done, b + 1)
                v.tensor_tensor(gb, tiles_ps[:, :, 0:D], gb, ALU.add).then_inc(rows_mixed, 1)
                v.tensor_scalar(mask[:].rearrange("p (a q) -> p a q", a=2), deg_ps, 1.0, None, ALU.add).then_inc(dve_step, 1)
                v.tensor_tensor(zb, tiles_ps[:, :, D:2 * D], zb, ALU.add)
                dve.wait_ge(dve_step, V1 * b + 1)
                v.tensor_scalar(deg, mask[:], TINY, None, ALU.max).then_inc(dve_step, 1)
                dve.wait_ge(dve_step, V1 * b + 2)
                v.tensor_scalar(mask[:], mask[:], 0.0, None, ALU.is_gt).then_inc(dve_step, 1)
                dve.wait_ge(squared, b + 1)
                v.reduce_sum(sums[:], squares[:], AX_X).then_inc(dve_step, 1)
                dve.wait_ge(dve_step, V1 * b + 4)
                v.tensor_scalar(stat[:, 0:BT], sums[:], 1.0 / D, EPS, ALU.mult, ALU.add
                                ).then_inc(stat_ready, 1)
                dve.wait_ge(rooted, b + 1)
                inverse_root(2 * BT, V1 * b + 4)
                v.tensor_tensor(dinv[:, bass.ds(BT * b, BT)], rb[:, BT:2 * BT], mask[:], ALU.mult
                                ).then_inc(dve_step, 1)
                v.tensor_tensor(gb, gb, over_features(rb[:, 0:BT]), ALU.mult)
                dve.wait_ge(dve_step, V1 * b + 10)
                v.tensor_tensor(gain[:], dinv[:, bass.ds(BT * b, BT)], rb[:, 0:BT], ALU.mult
                                ).then_inc(dve_step, 1)
                dve.wait_ge(dve_step, V1 * b + 11)
                v.tensor_tensor(zb, zb, over_features(gain[:]), ALU.mult).then_inc(z_ready, 1)

            dve.wait_ge(z_ready, BLOCKS)
            with dve.Fori(0, BLOCKS) as b:
                row_tile = dve.snap(b * -BT + (BLOCKS - 1) * BT)
                gb = g[:, bass.ds(row_tile, BT), :]
                zb = z[:, bass.ds(row_tile, BT), :]
                db = dinv[:, bass.ds(row_tile, BT)]
                dve.wait_ge(tiles_done, b + (BLOCKS + 1))
                v.tensor_tensor(mixed[:], tiles_ps[:, :, 0:D], zb, ALU.add).then_inc(dve_step, 1)
                dve.wait_ge(dve_step, V2 * b + (S2 + 1))
                v.tensor_tensor(mixed[:], mixed[:], over_features(db), ALU.mult
                                ).then_inc(dve_step, 1)
                dve.wait_ge(dve_step, V2 * b + (S2 + 2))
                v.tensor_tensor(mixed[:], mixed[:], gb, ALU.add).then_inc(rows_mixed, 1)
                dve.wait_ge(squared, b + (BLOCKS + 1))
                v.reduce_sum(sums[:], squares[:], AX_X).then_inc(dve_step, 1)
                dve.wait_ge(dve_step, V2 * b + (S2 + 3))
                v.tensor_scalar(stat[:, 0:BT], sums[:], 1.0 / D, EPS, ALU.mult, ALU.add
                                ).then_inc(stat_ready, 1)
                dve.wait_ge(rooted, b + (BLOCKS + 1))
                inverse_root(BT, V2 * b + (S2 + 3))
                v.tensor_tensor(out_sb[:], mixed[:], over_features(rb[:, 0:BT]), ALU.mult
                                ).then_inc(out_ready, 1)


def kernel(x, adj, L0_gnn_weight, L1_gnn_W):
    import numpy as np
    import concourse.bacc as bacc
    from concourse.bass_utils import run_bass_kernel_spmd

    N, D = x.shape
    blocks, chunks = N // BLOCK, N // P // CHUNK_TILES
    both_halves = lambda a: np.ascontiguousarray(np.concatenate([a, a], axis=0))

    adj = np.asarray(adj).reshape(blocks, BLOCK, chunks, CHUNK_TILES, P)
    adj_chunks = np.ascontiguousarray(adj.transpose(0, 2, 4, 3, 1)).reshape(
        blocks * chunks, P, CHUNK_TILES, BLOCK)
    xT = np.asarray(x).T
    xT_halves = np.concatenate([xT[:, :N // 2], xT[:, N // 2:]], axis=0)
    w0, w1 = np.asarray(L0_gnn_weight), np.asarray(L1_gnn_W)
    weights = both_halves(np.concatenate([w0.T, w1.T, w1], axis=1))
    expand = np.eye(D, dtype=np.float32)
    expand[:, D - 1] = -1.0
    expand[D - 1, :] = 0.0
    ident = np.eye(D, dtype=np.float32)
    cent = ident - np.float32(1.0 / D)
    consts = both_halves(np.concatenate([cent, ident, expand, expand.T], axis=1))

    arrays = {"adj_chunks": adj_chunks, "xT_halves": np.ascontiguousarray(xT_halves),
              "weights": weights, "consts": consts}
    nc = bacc.Bacc("TRN2", target_bir_lowering=False, num_devices=1)
    args = [nc.dram_tensor(name, a.shape, F32, kind="ExternalInput").ap()
            for name, a in arrays.items()]
    out = nc.dram_tensor("out", (blocks, P, BLOCK // P, D), F32, kind="ExternalOutput").ap()
    two_layers(nc, *args, out)
    r = run_bass_kernel_spmd(nc, [arrays], core_ids=[0])
    got = r.results[0]["out"].reshape(blocks, P, BLOCK // P, D)
    return np.ascontiguousarray(got.transpose(0, 2, 1, 3)).reshape(N, D)
```

```python
from contextlib import ExitStack

import concourse.bass as bass
from concourse import mybir

F32 = mybir.dt.float32
ALU = mybir.AluOpType
ACT = mybir.ActivationFunctionType
AX_X = mybir.AxisListType.X

P = 128
EPS = 1e-5
TINY = 1.1754944e-38
CHUNK_TILES = 2
SLOTS = 19
X_SLOTS = 2
S_BANKS = 3
TURN_LAG = 2
KEPT_LAG = 7
X_LOADS = 4
COLS = 512
BLOCK = 2 * COLS
GROUP = 4


def again_after(b, blocks):
    middle = blocks - 3
    if b == middle:
        return [(t, range(t + 2, middle + 1)) for t in range(middle - 1)]
    if b == blocks - 1:
        return [(t, range(max(middle + 1, t + 2), blocks)) for t in range(blocks - 2)]
    return []


def make_plan(blocks, per_block):
    steps, turning = [], []
    uses_left = {}

    def chunks(j):
        return range(j * per_block, (j + 1) * per_block)

    def turn():
        if turning:
            steps.append(("turn", *turning.pop()))

    def end(layer, b, final):
        turn()
        steps.append(("end", layer, b, final))
        turning.append((layer, b, final))
        uses_left[turn] = TURN_LAG

    def stream(kind, b, c):
        for step in list(uses_left):
            uses_left[step] -= 1
            if uses_left[step] < 0:
                del uses_left[step]
                step()
        steps.append(("use", kind, b, c))

    def kept_of(b):
        def kept():
            for c in chunks(b):
                steps.append(("use", "kept", b, c))
            if b:
                for c in chunks(b):
                    steps.append(("use", "kept", b - 1, c))
                end(2, b - 1, b == blocks - 1)
            if b == blocks - 1:
                uses_left[lambda: end(2, b, True)] = 2 * TURN_LAG
        return kept

    for b in range(blocks):
        order = [*range(b - 1), *range(b + 2, blocks), b - 1, b + 1, b]
        for j in order:
            for c in chunks(j) if 0 <= j < blocks else ():
                stream("both" if j < b else "one", b, c)
        end(1, b, False)
        uses_left[kept_of(b)] = KEPT_LAG
        for t, js in again_after(b, blocks):
            for j in js:
                for c in chunks(j):
                    stream("again", t, c)
            end(2, t, b == blocks - 1)
    turn()
    return steps


def place_loads(uses):
    last = {(b, c): n for n, (kind, b, c) in enumerate(uses) if kind == "kept"}
    free = [(0 if s < SLOTS - X_SLOTS else 1, s) for s in range(SLOTS)]
    loads, load_of, current, count = [], [], {}, [0] * SLOTS
    for n, (kind, b, c) in enumerate(uses):
        if kind != "kept":
            free.sort()
            after, s = free.pop(0)
            assert after <= n
            count[s] += 1
            current[b, c] = len(loads)
            loads.append((b, c, s, count[s], after))
            free.append((last[b, c] + 1 if kind == "one" and (b, c) in last else n + 1, s))
        load_of.append(current[b, c])
    return loads, load_of


def place_sums(plan):
    parts, banks, freed_by = [], [], [0] * (1 + S_BANKS)
    bank_of, free, latest = {}, list(range(1, 1 + S_BANKS)), {}
    for step in plan:
        if step[0] == "use":
            _, kind, b, _ = step
            here = []
            for layer in {"one": (1,), "both": (2, 1)}.get(kind, (2,)):
                first = (layer, b) not in bank_of
                if first:
                    bank_of[layer, b] = 0 if layer == 1 else free.pop(0)
                bank = bank_of[layer, b]
                here.append([layer, bank, first, False, freed_by[bank] if first else 0])
                latest[layer, b] = here[-1]
            parts.append(here)
        elif step[0] == "end":
            bank = bank_of.pop(step[1:3])
            latest.pop(step[1:3])[3] = True
            banks.append(bank)
            freed_by[bank] = len(banks)
            if bank:
                free.append(bank)
    return parts, banks


def two_layers(nc, adj_chunks, xT_halves, weights, consts, identity, out):
    n_chunks = adj_chunks.shape[0]
    D = weights.shape[1] // 2
    N = 2 * xT_halves.shape[1]
    BLOCKS = N // BLOCK
    TILES = N // P
    BT = BLOCK // P
    HT = BT // 2
    CHUNKS = TILES // CHUNK_TILES
    GROUPS = TILES // GROUP
    assert 2 * D == P and n_chunks == CHUNKS * BLOCKS

    plan = make_plan(BLOCKS, CHUNKS // BLOCKS)
    loads, load_of = place_loads([step[1:] for step in plan if step[0] == "use"])
    parts, banks = place_sums(plan)
    turns = [step[1:] for step in plan if step[0] == "turn"]
    uses_by_end = [sum(earlier[0] == "use" for earlier in plan[:n])
                   for n, step in enumerate(plan) if step[0] == "end"]

    with ExitStack() as ctx:
        def sb(name, shape):
            return ctx.enter_context(nc.sbuf_tensor(name, shape, F32))

        def psum(name, shape):
            return ctx.enter_context(nc.psum_tensor(name, shape, F32))

        def sem(name):
            return ctx.enter_context(nc.semaphore(name))

        slots = sb("slots", [P, SLOTS, CHUNK_TILES, BLOCK])
        xT = slots[:, SLOTS - X_SLOTS:SLOTS].rearrange("p s k i -> p (s k i)")
        ident = sb("ident", [P, D])
        from_agg = sb("from_agg", [P, 2 * D])
        y = sb("y", [P, TILES, D])
        g = sb("g", [P, TILES, D])
        z = sb("z", [P, TILES, D])
        dinv = sb("dinv", [P, TILES])
        agg_sb = sb("agg_sb", [P, COLS])
        mixed = sb("mixed", [P, BT, D])
        squares = sb("squares", [P, BT, D])
        out_sb = squares
        early = mixed[:].rearrange("p t d -> p (t d)")
        w_sb, w1c, from_x = early[:, 0:2 * D], early[:, 2 * D:3 * D], early[:, 3 * D:6 * D]
        c_sb = squares[:].rearrange("p t d -> p (t d)")[:, 0:3 * D]
        sums = sb("sums", [P, BT])
        stat = sb("stat", [P, 2 * BT])
        root = sb("root", [P, 2 * BT])
        rs = sb("rs", [P, 2 * BT])
        ra = sb("ra", [P, 2 * BT])
        rb = sb("rb", [P, 2 * BT])
        mask = sb("mask", [P, BT])
        eps = sb("eps", [P, 1])
        gain = sb("gain", [P, BT])

        cent, expand, expandT = c_sb[:, 0:D], c_sb[:, D:2 * D], c_sb[:, 2 * D:3 * D]
        w0T, w1T = w_sb[:, 0:D], w_sb[:, D:2 * D]

        sums_ps = psum("sums_ps", [P, 1 + S_BANKS, COLS])
        fold_ps = sums_ps[:, 0]
        turn_ps = psum("turn_ps", [P, 4 * COLS])
        x_ps = turn_ps[:].rearrange("p (g k c) -> p g k c", g=2, k=GROUP)
        tiles_ps = turn_ps[:, 0:2 * COLS].rearrange("p (t c) -> p t c", c=P)
        halves_ps = turn_ps[:, 2 * COLS:4 * COLS].rearrange("p (a c) -> p a c", a=2)
        rows_ps = [halves_ps[:, a, 0:HT * D].rearrange("p (q d) -> p q d", d=D) for a in range(2)]
        deg_ps = halves_ps[:, :, HT * D:HT * D + HT]

        weights_loaded = sem("weights_loaded")
        x_loaded = [sem(f"x_loaded{i}") for i in range(X_LOADS)]
        slot_loaded = [sem(f"slot_loaded{s}") for s in range(SLOTS)]
        chunk_used = sem("chunk_used")
        folds_done = sem("folds_done")
        folds_copied = sem("folds_copied")
        consts_copied = sem("consts_copied")
        y_ones = sem("y_ones")
        eps_set = sem("eps_set")
        x_products = sem("x_products")
        x_copied = [sem(f"x_copied_by_{e}") for e in ("scalar", "vector")]
        agg_copied = sem("agg_copied")
        halves_turned = sem("halves_turned")
        rows_read = sem("rows_read")
        rows_mixed = sem("rows_mixed")
        squared = sem("squared")
        stat_ready = sem("stat_ready")
        rooted = sem("rooted")
        z_ready = sem("z_ready")
        halves_mixed = sem("halves_mixed")
        halves_squared = sem("halves_squared")
        sums_ready = sem("sums_ready")
        out_ready = sem("out_ready")
        out_stored = sem("out_stored")
        dve_step = sem("dve_step")

        block = ctx.enter_context(nc.Block())

        @block.sync
        def _(sp):
            sp.dma_start(w_sb, weights).then_inc(weights_loaded, 16)
            sp.dma_start(c_sb, consts).then_inc(weights_loaded, 16)
            sp.dma_start(ident[:], identity).then_inc(weights_loaded, 16)
            for i in range(X_LOADS):
                part = slice(i * N // 2 // X_LOADS, (i + 1) * N // 2 // X_LOADS)
                sp.dma_start(xT[:, part], xT_halves[:, part]).then_inc(x_loaded[i], 16)
            waited = 0
            for b, c, s, _, after in loads:
                if after > waited:
                    sp.wait_ge(chunk_used, after)
                    waited = after
                sp.dma_start(slots[:, s], adj_chunks[b * CHUNKS + c]).then_inc(slot_loaded[s], 16)

        @block.tensor
        def _(pe):
            pe.wait_ge(weights_loaded, 48)
            for a in range(2):
                lo, hi = D * a, D * a + D
                pe.matmul(fold_ps[lo:hi, 0:D], w0T[lo:hi], cent[lo:hi], start=True, stop=True)
                mm = pe.matmul(fold_ps[lo:hi, D:2 * D], w1T[lo:hi], cent[lo:hi], start=True, stop=True)
            mm.then_inc(folds_done, 1)
            pe.wait_ge(folds_copied, 1)
            for a in range(2):
                lo, hi = D * a, D * a + D
                pe.matmul(fold_ps[lo:hi, 2 * D:3 * D], cent[lo:hi], w1c[lo:hi], start=True, stop=True)
                mm = pe.matmul(fold_ps[lo:hi, 3 * D:4 * D], expandT[lo:hi], w1c[lo:hi],
                               start=True, stop=True)
            mm.then_inc(folds_done, 1)

            pe.wait_ge(folds_copied, 2)
            pe.wait_ge(consts_copied, 1)
            for q in range(GROUPS):
                if q % (GROUPS // 2) % (GROUPS // 2 // X_LOADS) == 0:
                    pe.wait_ge(x_loaded[q % (GROUPS // 2) // (GROUPS // 2 // X_LOADS)], 16)
                if q >= 2:
                    pe.wait_ge(x_copied[q % 2], q // 2)
                for k in range(GROUP):
                    a, col = divmod((q * GROUP + k) * P, N // 2)
                    mm = pe.matmul(x_ps[:, q % 2, k, 0:3 * D], xT[D * a:D * a + D, col:col + P],
                                   from_x[D * a:D * a + D, :], start=True, stop=True)
                mm.then_inc(x_products, 1)
            for reader in x_copied:
                pe.wait_ge(reader, GROUPS // 2)
            pe.wait_ge(y_ones, 1)

            def add_chunk(stationary, sums, s, c, first, last):
                for k in range(CHUNK_TILES):
                    for a in range(2):
                        mm = pe.matmul(sums[D * a:D * a + D, :],
                                       stationary[:, c * CHUNK_TILES + k, :],
                                       slots[:, s, k, COLS * a:COLS * a + COLS],
                                       start=first and k == 0, stop=last and k == CHUNK_TILES - 1)
                return mm

            def turn_one():
                for a in range(2):
                    for q in range(HT):
                        part = agg_sb[D * a:D * a + D, q * P:(q + 1) * P]
                        pe.matmul(tiles_ps[:, a * HT + q, :], part, from_agg[D * a:D * a + D, :],
                                  start=True, stop=True)
                        mm = pe.matmul(deg_ps[:, a, q:q + 1], part,
                                       ident[D * a:D * a + D, D - 1:D], start=True, stop=True)
                    mm.then_inc(halves_turned, 1)

            def turn_two():
                for a in range(2):
                    for q in range(HT):
                        mm = pe.matmul(rows_ps[a][:, q, :],
                                       agg_sb[D * a:D * a + D, q * P:(q + 1) * P],
                                       ident[D * a:D * a + D, :], start=True, stop=True)
                    mm.then_inc(halves_turned, 1)

            n_use = n_turn = n_loaded = z_known = 0
            for step in plan:
                if step[0] == "use":
                    c, load = step[3], load_of[n_use]
                    _, _, s, nth, _ = loads[load]
                    if load == n_loaded:
                        pe.wait_ge(slot_loaded[s], 16 * nth)
                        n_loaded += 1
                    for layer, bank, first, last, copied in parts[n_use]:
                        if layer == 2 and c * CHUNK_TILES // BT == z_known:
                            z_known += 1
                            pe.wait_ge(z_ready, z_known)
                        if copied:
                            pe.wait_ge(agg_copied, copied)
                        mm = add_chunk(z if layer == 2 else y, sums_ps[:, bank], s, c, first, last)
                    mm.then_inc(chunk_used, 1)
                    n_use += 1
                elif step[0] == "turn":
                    n_turn += 1
                    pe.wait_ge(agg_copied, n_turn)
                    if n_turn > 1:
                        pe.wait_ge(rows_read, n_turn - 1)
                    if step[1] == 1:
                        turn_one()
                    else:
                        turn_two()

        @block.scalar
        def _(act):
            act.wait_ge(weights_loaded, 48)
            nc.scalar.copy(from_x[:, D:2 * D], cent)
            nc.scalar.copy(from_agg[:, 0:D], expand).then_inc(consts_copied, 1)

            for q in range(0, GROUPS, 2):
                act.wait_ge(x_products, q + 1)
                rows = slice(q * GROUP, (q + 1) * GROUP)
                nc.scalar.copy(y[:, rows, 0:D - 1], x_ps[:, 0, :, 0:D - 1])
                nc.scalar.copy(g[:, rows, :], x_ps[:, 0, :, D:2 * D])
                nc.scalar.copy(z[:, rows, :], x_ps[:, 0, :, 2 * D:3 * D]).then_inc(x_copied[0], 1)

            act.wait_ge(eps_set, 1)
            n_one = n_final = 0
            for n, (layer, b, final) in enumerate(turns):
                act.wait_ge(chunk_used, uses_by_end[n])
                if n:
                    act.wait_ge(halves_turned, 2 * n)
                nc.scalar.copy(agg_sb[:], sums_ps[:, banks[n]]).then_inc(agg_copied, 1)
                if layer == 1:
                    n_one += 1
                    act.wait_ge(rows_mixed, n_one)
                    nc.scalar.activation(squares[:], g[:, b * BT:(b + 1) * BT, :], ACT.Square
                                         ).then_inc(squared, 1)
                    act.wait_ge(stat_ready, n_one)
                    nc.scalar.activation(root[:], stat[:], ACT.Sqrt).then_inc(rooted, 1)
                if final:
                    n_final += 1
                    if n_final > 1:
                        act.wait_ge(out_stored, 16 * (n_final - 1))
                    for a in range(2):
                        tiles = slice(a * HT, (a + 1) * HT)
                        act.wait_ge(halves_mixed, 2 * (n_final - 1) + a + 1)
                        nc.scalar.activation(squares[:, tiles], mixed[:, tiles], ACT.Square
                                             ).then_inc(halves_squared, 1)
                    act.wait_ge(sums_ready, 2 * n_final)
                    nc.scalar.activation(root[:, 0:BT], sums[:], ACT.Sqrt, scale=1.0 / D,
                                         bias=eps[:, 0:1]).then_inc(rooted, 1)
                    act.wait_ge(out_ready, n_final)
                    act.dma_start(out[b], out_sb[:]).then_inc(out_stored, 16)
            act.wait_ge(out_stored, 16 * BLOCKS)

        @block.vector
        def _(dve):
            v = nc.vector
            steps = [0]

            def link(instruction):
                steps[0] += 1
                instruction.then_inc(dve_step, 1)
                dve.wait_ge(dve_step, steps[0])

            def inverse_root(n):
                link(v.reciprocal(rs[:, 0:n], root[:, 0:n]))
                link(v.scalar_tensor_tensor(out=ra[:, 0:n], in0=stat[:, 0:n], scalar=-0.5,
                                            in1=rs[:, 0:n], op0=ALU.mult, op1=ALU.mult))
                link(v.tensor_tensor(ra[:, 0:n], ra[:, 0:n], rs[:, 0:n], ALU.mult))
                link(v.scalar_tensor_tensor(out=rb[:, 0:n], in0=ra[:, 0:n], scalar=1.5,
                                            in1=rs[:, 0:n], op0=ALU.add, op1=ALU.mult))

            def over_features(column):
                return column.unsqueeze(2).to_broadcast([P, column.shape[1], D])

            v.memset(y[:, :, D - 1:D], 1.0).then_inc(y_ones, 1)
            v.memset(eps[:], EPS).then_inc(eps_set, 1)
            dve.wait_ge(folds_done, 1)
            v.tensor_copy(from_x[:, 0:D], fold_ps[:, 0:D])
            v.tensor_copy(w1c[:], fold_ps[:, D:2 * D]).then_inc(folds_copied, 1)
            dve.wait_ge(folds_done, 2)
            v.tensor_copy(from_x[:, 2 * D:3 * D], fold_ps[:, 2 * D:3 * D])
            v.tensor_copy(from_agg[:, D:2 * D], fold_ps[:, 3 * D:4 * D]).then_inc(folds_copied, 1)

            for q in range(1, GROUPS, 2):
                dve.wait_ge(x_products, q + 1)
                rows = slice(q * GROUP, (q + 1) * GROUP)
                v.tensor_copy(y[:, rows, 0:D - 1], x_ps[:, 1, :, 0:D - 1])
                v.tensor_copy(g[:, rows, :], x_ps[:, 1, :, D:2 * D])
                v.tensor_copy(z[:, rows, :], x_ps[:, 1, :, 2 * D:3 * D]).then_inc(x_copied[1], 1)
            for reader in x_copied:
                dve.wait_ge(reader, GROUPS // 2)

            deg = stat[:, BT:2 * BT]
            n_one = n_final = 0
            for n, (layer, b, final) in enumerate(turns):
                gb, zb, db = (t[:, b * BT:(b + 1) * BT] for t in (g, z, dinv))
                if layer == 1:
                    n_one += 1
                    dve.wait_ge(halves_turned, 2 * n + 2)
                    v.tensor_tensor(gb, tiles_ps[:, :, 0:D], gb, ALU.add).then_inc(rows_mixed, 1)
                    link(v.tensor_scalar(mask[:].rearrange("p (a q) -> p a q", a=2), deg_ps, 1.0,
                                         None, ALU.add))
                    v.tensor_tensor(zb, tiles_ps[:, :, D:2 * D], zb, ALU.add).then_inc(rows_read, 1)
                    link(v.tensor_scalar(deg, mask[:], TINY, None, ALU.max))
                    link(v.tensor_scalar(mask[:], mask[:], 0.0, None, ALU.is_gt))
                    dve.wait_ge(squared, n_one)
                    link(v.reduce_sum(sums[:], squares[:], AX_X))
                    v.tensor_scalar(stat[:, 0:BT], sums[:], 1.0 / D, EPS, ALU.mult, ALU.add
                                    ).then_inc(stat_ready, 1)
                    dve.wait_ge(rooted, n_one + n_final)
                    inverse_root(2 * BT)
                    link(v.tensor_tensor(db, rb[:, BT:2 * BT], mask[:], ALU.mult))
                    link(v.tensor_tensor(gain[:], db, rb[:, 0:BT], ALU.mult))
                    v.tensor_tensor(zb, zb, over_features(gain[:]), ALU.mult).then_inc(z_ready, 1)
                    link(v.tensor_tensor(gb, gb, over_features(rb[:, 0:BT]), ALU.mult))
                    dve.wait_ge(z_ready, n_one)
                    link(v.tensor_tensor(mixed[:], zb, over_features(db), ALU.mult))
                    link(v.tensor_tensor(gb, mixed[:], gb, ALU.add))
                    continue
                for a in range(2):
                    tiles = slice(a * HT, (a + 1) * HT)
                    dve.wait_ge(halves_turned, 2 * n + 1 + a)
                    scaled = v.tensor_tensor(mixed[:, tiles], rows_ps[a],
                                             over_features(db[:, tiles]), ALU.mult)
                    if a == 0:
                        link(scaled)
                    else:
                        scaled.then_inc(rows_read, 1)
                        dve.wait_ge(rows_read, n + 1)
                    if final:
                        v.tensor_tensor(mixed[:, tiles], mixed[:, tiles], gb[:, tiles], ALU.add
                                        ).then_inc(halves_mixed, 1)
                    else:
                        link(v.tensor_tensor(gb[:, tiles], mixed[:, tiles], gb[:, tiles], ALU.add))
                if not final:
                    continue
                n_final += 1
                for a in range(2):
                    tiles = slice(a * HT, (a + 1) * HT)
                    dve.wait_ge(halves_squared, 2 * (n_final - 1) + a + 1)
                    v.reduce_sum(sums[:, tiles], squares[:, tiles], AX_X).then_inc(sums_ready, 1)
                dve.wait_ge(sums_ready, 2 * n_final)
                link(v.tensor_scalar(stat[:, 0:BT], sums[:], 1.0 / D, EPS, ALU.mult, ALU.add))
                dve.wait_ge(rooted, n_one + n_final)
                inverse_root(BT)
                v.tensor_tensor(out_sb[:], mixed[:], over_features(rb[:, 0:BT]), ALU.mult
                                ).then_inc(out_ready, 1)
                dve.wait_ge(out_ready, n_final)


def kernel(x, adj, L0_gnn_weight, L1_gnn_W):
    import numpy as np
    import concourse.bacc as bacc
    from concourse.bass_utils import run_bass_kernel_spmd

    N, D = x.shape
    blocks, chunks = N // BLOCK, N // P // CHUNK_TILES
    both_halves = lambda a: np.ascontiguousarray(np.concatenate([a, a], axis=0))

    adj = np.asarray(adj).reshape(blocks, BLOCK, chunks, CHUNK_TILES, P)
    adj_chunks = np.ascontiguousarray(adj.transpose(0, 2, 4, 3, 1)).reshape(
        blocks * chunks, P, CHUNK_TILES, BLOCK)
    xT = np.asarray(x).T
    xT_halves = np.concatenate([xT[:, :N // 2], xT[:, N // 2:]], axis=0)
    w0, w1 = np.asarray(L0_gnn_weight), np.asarray(L1_gnn_W)
    weights = both_halves(np.concatenate([w0.T, w1.T], axis=1))
    expand = np.eye(D, dtype=np.float32)
    expand[:, D - 1] = -1.0
    expand[D - 1, :] = 0.0
    ident = np.eye(D, dtype=np.float32)
    cent = ident - np.float32(1.0 / D)
    consts = both_halves(np.concatenate([cent, expand, expand.T], axis=1))

    arrays = {"adj_chunks": adj_chunks, "xT_halves": np.ascontiguousarray(xT_halves),
              "weights": weights, "consts": consts, "identity": both_halves(ident)}
    nc = bacc.Bacc("TRN2", target_bir_lowering=False, num_devices=1)
    args = [nc.dram_tensor(name, a.shape, F32, kind="ExternalInput").ap()
            for name, a in arrays.items()]
    out = nc.dram_tensor("out", (blocks, P, BLOCK // P, D), F32, kind="ExternalOutput").ap()
    two_layers(nc, *args, out)
    r = run_bass_kernel_spmd(nc, [arrays], core_ids=[0])
    got = r.results[0]["out"].reshape(blocks, P, BLOCK // P, D)
    return np.ascontiguousarray(got.transpose(0, 2, 1, 3)).reshape(N, D)
```

```python
from contextlib import ExitStack

import concourse.bass as bass
from concourse import mybir

F32 = mybir.dt.float32
ALU = mybir.AluOpType
ACT = mybir.ActivationFunctionType
AX_X = mybir.AxisListType.X

P = 128
EPS = 1e-5
TINY = 1.1754944e-38
CHUNK_TILES = 2
SLOTS = 17
X_SLOTS = 2
PAIRS = 3
TURN_LAG = 2
KEPT_LAG = 6
AGAIN_FROM = 10
X_LOADS = 4
COLS = 512
BLOCK = 2 * COLS
GROUP = 4


def again_in(b, blocks):
    mixed_in = {blocks - 3: (0,), blocks - 2: (1, 2), blocks - 1: (3,)}
    if b < blocks:
        return [(t, range(t + 2, b)) for t in mixed_in.get(b, ())]
    by_then = {t: first for first, ts in mixed_in.items() for t in ts}
    return [(t, range(by_then.get(t, t + 2), blocks)) for t in range(blocks - 2)]


def make_plan(blocks, per_block):
    steps, turning = [], []
    uses_left = {}

    def chunks(j):
        return range(j * per_block, (j + 1) * per_block)

    def turn():
        if turning:
            steps.append(("turn", *turning.pop()))

    def end(layer, b, final):
        turn()
        steps.append(("end", layer, b, final))
        turning.append((layer, b, final))
        uses_left[turn] = TURN_LAG

    def stream(kind, b, c):
        for step in list(uses_left):
            uses_left[step] -= 1
            if uses_left[step] < 0:
                del uses_left[step]
                step()
        steps.append(("use", kind, b, c))

    def kept_of(b):
        def kept():
            for c in chunks(b):
                steps.append(("use", "kept", b, c))
            if b:
                for c in chunks(b):
                    steps.append(("use", "kept", b - 1, c))
                end(2, b - 1, b == blocks - 1)
            if b == blocks - 1:
                uses_left[lambda: end(2, b, True)] = 2 * TURN_LAG
        return kept

    for b in range(blocks):
        order = [*range(b - 1), *range(b + 2, blocks), b - 1, b + 1, b]
        mine = [(j, c) for j in order if 0 <= j < blocks for c in chunks(j)]
        again = [(t, c, c == chunks(js[-1])[-1])
                 for t, js in again_in(b, blocks) for j in js for c in chunks(j)]
        spread = len(mine) - 1 - AGAIN_FROM
        done = 0
        for n, (j, c) in enumerate(mine):
            stream("both" if j < b else "one", b, c)
            due = min(len(again), max(0, n + 1 - AGAIN_FROM) * len(again) // spread)
            for t, c_again, last in again[done:due]:
                stream("again", t, c_again)
                if last:
                    end(2, t, False)
            done = due
        end(1, b, False)
        uses_left[kept_of(b)] = KEPT_LAG
    for t, js in again_in(blocks, blocks):
        for j in js:
            for c in chunks(j):
                stream("again", t, c)
        end(2, t, True)
    turn()
    return steps


def place_loads(uses):
    last = {(b, c): n for n, (kind, b, c) in enumerate(uses) if kind == "kept"}
    free = [(0 if s < SLOTS - X_SLOTS else 1, s) for s in range(SLOTS)]
    loads, load_of, current, count = [], [], {}, [0] * SLOTS
    for n, (kind, b, c) in enumerate(uses):
        if kind != "kept":
            free.sort()
            after, s = free.pop(0)
            assert after <= n
            count[s] += 1
            current[b, c] = len(loads)
            loads.append((b, c, s, count[s], after))
            free.append((last[b, c] + 1 if kind == "one" and (b, c) in last else n + 1, s))
        load_of.append(current[b, c])
    return loads, load_of


def place_sums(plan):
    parts, pairs, pair_of, latest = [], [], {}, {}
    free = [(0, pair) for pair in range(PAIRS)]

    def add(layers, owner, copied):
        first = (layers[0], owner) not in latest
        parts[-1].append([layers, pair_of[owner], first, False, copied])
        for layer in layers:
            latest[layer, owner] = parts[-1][-1]

    for step in plan:
        if step[0] == "use":
            _, kind, b, _ = step
            owner, copied = (kind == "again", b), 0
            if owner not in pair_of:
                copied, pair_of[owner] = free.pop(0)
            parts.append([])
            begun = [(layer, owner) in latest for layer in (1, 2)]
            if kind != "both":
                add((1,) if kind == "one" else (2,), owner, copied)
            elif begun[0] == begun[1]:
                add((1, 2), owner, copied)
            else:
                add((1,), owner, copied)
                add((2,), owner, 0)
        elif step[0] == "end":
            _, layer, b, _ = step
            owner = (True, b) if (True, b) in pair_of and layer == 2 else (False, b)
            pairs.append(pair_of[owner])
            part = latest.pop((layer, owner))
            assert part[0] == (layer,)
            part[3] = True
            if layer == 2:
                free.append((len(pairs), pair_of.pop(owner)))
                free.sort()
    return parts, pairs


def two_layers(nc, adj_chunks, xT_halves, weights, consts, identity, out):
    n_chunks = adj_chunks.shape[0]
    D = weights.shape[1] // 2
    N = 2 * xT_halves.shape[1]
    BLOCKS = N // BLOCK
    TILES = N // P
    BT = BLOCK // P
    HT = BT // 2
    CHUNKS = TILES // CHUNK_TILES
    GROUPS = TILES // GROUP
    assert 2 * D == P and n_chunks == CHUNKS * BLOCKS

    plan = make_plan(BLOCKS, CHUNKS // BLOCKS)
    loads, load_of = place_loads([step[1:] for step in plan if step[0] == "use"])
    parts, pairs = place_sums(plan)
    turns = [step[1:] for step in plan if step[0] == "turn"]
    uses_by_end = [sum(earlier[0] == "use" for earlier in plan[:n])
                   for n, step in enumerate(plan) if step[0] == "end"]

    with ExitStack() as ctx:
        def sb(name, shape):
            return ctx.enter_context(nc.sbuf_tensor(name, shape, F32))

        def psum(name, shape):
            return ctx.enter_context(nc.psum_tensor(name, shape, F32))

        def sem(name):
            return ctx.enter_context(nc.semaphore(name))

        slots = sb("slots", [P, SLOTS, CHUNK_TILES, BLOCK])
        xT = slots[:, SLOTS - X_SLOTS:SLOTS].rearrange("p s k i -> p (s k i)")
        ident = sb("ident", [P, D])
        from_agg = sb("from_agg", [P, 2 * D])
        yzy = sb("yzy", [P, TILES, 3, D])
        y, y_again = yzy[:, :, 0, :], yzy[:, :, 2, :]
        z = yzy[:, :, 1, :]
        g = sb("g", [P, TILES, D])
        dinv = sb("dinv", [P, TILES])
        agg_sb = sb("agg_sb", [P, COLS])
        mixed = sb("mixed", [P, BT, D])
        squares = sb("squares", [P, BT, D])
        early = mixed[:].rearrange("p t d -> p (t d)")
        w_sb, w1c, from_x = early[:, 0:2 * D], early[:, 2 * D:3 * D], early[:, 3 * D:6 * D]
        c_sb = squares[:].rearrange("p t d -> p (t d)")[:, 0:3 * D]
        sums = sb("sums", [P, BT])
        stat = sb("stat", [P, 2 * BT])
        root = sb("root", [P, 2 * BT])
        rs = sb("rs", [P, 2 * BT])
        ra = sb("ra", [P, 2 * BT])
        rb = sb("rb", [P, 2 * BT])
        mask = sb("mask", [P, BT])
        eps = sb("eps", [P, 1])
        gain = sb("gain", [P, BT])

        cent, expand, expandT = c_sb[:, 0:D], c_sb[:, D:2 * D], c_sb[:, 2 * D:3 * D]
        w0T, w1T = w_sb[:, 0:D], w_sb[:, D:2 * D]

        banks_ps = psum("banks_ps", [P, 2 * PAIRS + 2, COLS])
        fold_ps = banks_ps[:, 0]
        x_ps = banks_ps[:, 2 * PAIRS - 2:].rearrange("p (g b) (k c) -> p g (b k) c", g=2, k=2)
        turn_ps = banks_ps[:, 2 * PAIRS:]
        tiles_ps = turn_ps.rearrange("p a (q c) -> p (a q) c", c=P)
        rows_ps = [turn_ps[:, a, 0:HT * D].rearrange("p (q d) -> p q d", d=D) for a in range(2)]

        weights_loaded = sem("weights_loaded")
        x_loaded = [sem(f"x_loaded{i}") for i in range(X_LOADS)]
        slot_loaded = [sem(f"slot_loaded{s}") for s in range(SLOTS)]
        chunk_used = sem("chunk_used")
        folds_done = sem("folds_done")
        folds_copied = sem("folds_copied")
        consts_copied = sem("consts_copied")
        y_ones = sem("y_ones")
        eps_set = sem("eps_set")
        x_products = sem("x_products")
        x_copied = [sem(f"x_copied_by_{e}") for e in ("scalar", "vector")]
        y_doubled = sem("y_doubled")
        agg_copied = sem("agg_copied")
        halves_turned = sem("halves_turned")
        rows_read = sem("rows_read")
        rows_mixed = sem("rows_mixed")
        squared = sem("squared")
        stat_ready = sem("stat_ready")
        rooted = sem("rooted")
        z_ready = sem("z_ready")
        halves_mixed = sem("halves_mixed")
        halves_squared = sem("halves_squared")
        sums_ready = sem("sums_ready")
        out_ready = sem("out_ready")
        out_stored = sem("out_stored")
        dve_step = sem("dve_step")

        def half_of(layer, a):
            return slice(0, D) if (layer == 1) == (a == 0) else slice(D, P)

        block = ctx.enter_context(nc.Block())

        @block.sync
        def _(sp):
            sp.dma_start(w_sb, weights).then_inc(weights_loaded, 16)
            sp.dma_start(c_sb, consts).then_inc(weights_loaded, 16)
            sp.dma_start(ident[:], identity).then_inc(weights_loaded, 16)
            for i in range(X_LOADS):
                part = slice(i * N // 2 // X_LOADS, (i + 1) * N // 2 // X_LOADS)
                sp.dma_start(xT[:, part], xT_halves[:, part]).then_inc(x_loaded[i], 16)
            waited = 0
            for b, c, s, _, after in loads:
                if after > waited:
                    sp.wait_ge(chunk_used, after)
                    waited = after
                sp.dma_start(slots[:, s], adj_chunks[b * CHUNKS + c]).then_inc(slot_loaded[s], 16)

        @block.tensor
        def _(pe):
            pe.wait_ge(weights_loaded, 48)
            for a in range(2):
                lo, hi = D * a, D * a + D
                pe.matmul(fold_ps[lo:hi, 0:D], w0T[lo:hi], cent[lo:hi], start=True, stop=True)
                mm = pe.matmul(fold_ps[lo:hi, D:2 * D], w1T[lo:hi], cent[lo:hi], start=True, stop=True)
            mm.then_inc(folds_done, 1)
            pe.wait_ge(folds_copied, 1)
            for a in range(2):
                lo, hi = D * a, D * a + D
                pe.matmul(fold_ps[lo:hi, 2 * D:3 * D], cent[lo:hi], w1c[lo:hi], start=True, stop=True)
                mm = pe.matmul(fold_ps[lo:hi, 3 * D:4 * D], expandT[lo:hi], w1c[lo:hi],
                               start=True, stop=True)
            mm.then_inc(folds_done, 1)

            pe.wait_ge(folds_copied, 2)
            pe.wait_ge(consts_copied, 1)
            for q in range(GROUPS):
                if q % (GROUPS // 2) % (GROUPS // 2 // X_LOADS) == 0:
                    pe.wait_ge(x_loaded[q % (GROUPS // 2) // (GROUPS // 2 // X_LOADS)], 16)
                if q >= 2:
                    pe.wait_ge(x_copied[q % 2], q // 2)
                for k in range(GROUP):
                    a, col = divmod((q * GROUP + k) * P, N // 2)
                    mm = pe.matmul(x_ps[:, q % 2, k, 0:3 * D], xT[D * a:D * a + D, col:col + P],
                                   from_x[D * a:D * a + D, :], start=True, stop=True)
                mm.then_inc(x_products, 1)
            for reader in x_copied:
                pe.wait_ge(reader, GROUPS // 2)
            pe.wait_ge(y_ones, 1)

            def add_both(pair, s, c, first):
                for k in range(CHUNK_TILES):
                    for a in range(2):
                        mm = pe.matmul(banks_ps[:, 2 * pair + a, :],
                                       yzy[:, c * CHUNK_TILES + k, a:a + 2, :].rearrange(
                                           "p s d -> p (s d)"),
                                       slots[:, s, k, COLS * a:COLS * a + COLS],
                                       start=first and k == 0, stop=False)
                return mm

            def add_one(layer, pair, s, c, first, last):
                stationary = y if layer == 1 else z
                for k in range(CHUNK_TILES):
                    for a in range(2):
                        column_tile = half_of(layer, a)
                        mm = pe.matmul(banks_ps[column_tile, 2 * pair + a, :],
                                       stationary[:, c * CHUNK_TILES + k, :],
                                       slots[:, s, k, COLS * a:COLS * a + COLS],
                                       start=first and k == 0, stop=last and k == CHUNK_TILES - 1)
                return mm

            def turn(layer, n):
                for a in range(2):
                    pe.wait_ge(agg_copied, 2 * n + a + 1)
                    if n and a == 0:
                        pe.wait_ge(rows_read, n)
                    half = half_of(layer, a)
                    for q in range(HT):
                        part = agg_sb[half, q * P:(q + 1) * P]
                        if layer == 1:
                            mm = pe.matmul(tiles_ps[:, a * HT + q, :], part, from_agg[half, :],
                                           start=True, stop=True)
                        else:
                            mm = pe.matmul(rows_ps[a][:, q, :], part, ident[half, :],
                                           start=True, stop=True)
                    mm.then_inc(halves_turned, 1)

            n_use = n_turn = n_loaded = z_known = 0
            for step in plan:
                if step[0] == "use":
                    c, load = step[3], load_of[n_use]
                    _, _, s, nth, _ = loads[load]
                    if load == n_loaded:
                        pe.wait_ge(slot_loaded[s], 16 * nth)
                        n_loaded += 1
                    for layers, pair, first, last, copied in parts[n_use]:
                        if 2 in layers and c * CHUNK_TILES // BT == z_known:
                            if z_known == 0:
                                pe.wait_ge(y_doubled, 1)
                            z_known += 1
                            pe.wait_ge(z_ready, z_known)
                        if copied:
                            pe.wait_ge(agg_copied, 2 * copied)
                        if len(layers) == 2:
                            mm = add_both(pair, s, c, first)
                        else:
                            mm = add_one(layers[0], pair, s, c, first, last)
                    mm.then_inc(chunk_used, 1)
                    n_use += 1
                elif step[0] == "turn":
                    turn(step[1], n_turn)
                    n_turn += 1

        @block.scalar
        def _(act):
            act.wait_ge(weights_loaded, 48)
            nc.scalar.copy(from_x[:, D:2 * D], cent)
            nc.scalar.copy(from_agg[:, 2 * D - 1:2 * D], ident[:, D - 1:D])
            nc.scalar.copy(from_agg[:, 0:D], expand).then_inc(consts_copied, 1)

            for q in range(0, GROUPS, 2):
                act.wait_ge(x_products, q + 1)
                rows = slice(q * GROUP, (q + 1) * GROUP)
                nc.scalar.copy(y[:, rows, 0:D - 1], x_ps[:, 0, :, 0:D - 1])
                nc.scalar.copy(g[:, rows, :], x_ps[:, 0, :, D:2 * D])
                nc.scalar.copy(z[:, rows, :], x_ps[:, 0, :, 2 * D:3 * D]).then_inc(x_copied[0], 1)

            for writer in x_copied:
                act.wait_ge(writer, GROUPS // 2)
            act.wait_ge(y_ones, 1)
            nc.scalar.copy(y_again, y).then_inc(y_doubled, 1)

            act.wait_ge(eps_set, 1)
            n_one = n_final = 0
            for n, (layer, b, final) in enumerate(turns):
                act.wait_ge(chunk_used, uses_by_end[n])
                if n:
                    act.wait_ge(halves_turned, 2 * n)
                for a in range(2):
                    half = half_of(layer, a)
                    nc.scalar.copy(agg_sb[half, :], banks_ps[half, 2 * pairs[n] + a, :]
                                   ).then_inc(agg_copied, 1)
                if layer == 1:
                    n_one += 1
                    act.wait_ge(rows_mixed, n_one)
                    nc.scalar.activation(squares[:], g[:, b * BT:(b + 1) * BT, :], ACT.Square
                                         ).then_inc(squared, 1)
                    act.wait_ge(stat_ready, n_one)
                    nc.scalar.activation(root[:], stat[:], ACT.Sqrt).then_inc(rooted, 1)
                if final:
                    n_final += 1
                    for a in range(2):
                        tiles = slice(a * HT, (a + 1) * HT)
                        act.wait_ge(halves_mixed, 2 * (n_final - 1) + a + 1)
                        nc.scalar.activation(squares[:, tiles], mixed[:, tiles], ACT.Square
                                             ).then_inc(halves_squared, 1)
                    act.wait_ge(sums_ready, 2 * n_final)
                    nc.scalar.activation(root[:, 0:BT], sums[:], ACT.Sqrt, scale=1.0 / D,
                                         bias=eps[:, 0:1]).then_inc(rooted, 1)
                    act.wait_ge(out_ready, n_final)
                    act.dma_start(out[b], g[:, b * BT:(b + 1) * BT, :]).then_inc(out_stored, 16)
            act.wait_ge(out_stored, 16 * BLOCKS)

        @block.vector
        def _(dve):
            v = nc.vector
            steps = [0]

            def link(instruction):
                steps[0] += 1
                instruction.then_inc(dve_step, 1)
                dve.wait_ge(dve_step, steps[0])

            def inverse_root(n):
                link(v.reciprocal(rs[:, 0:n], root[:, 0:n]))
                link(v.scalar_tensor_tensor(out=ra[:, 0:n], in0=stat[:, 0:n], scalar=-0.5,
                                            in1=rs[:, 0:n], op0=ALU.mult, op1=ALU.mult))
                link(v.tensor_tensor(ra[:, 0:n], ra[:, 0:n], rs[:, 0:n], ALU.mult))
                link(v.scalar_tensor_tensor(out=rb[:, 0:n], in0=ra[:, 0:n], scalar=1.5,
                                            in1=rs[:, 0:n], op0=ALU.add, op1=ALU.mult))

            def over_features(column):
                return column.unsqueeze(2).to_broadcast([P, column.shape[1], D])

            v.memset(y[:, :, D - 1:D], 1.0).then_inc(y_ones, 1)
            v.memset(eps[:], EPS).then_inc(eps_set, 1)
            dve.wait_ge(folds_done, 1)
            v.tensor_copy(from_x[:, 0:D], fold_ps[:, 0:D])
            v.tensor_copy(w1c[:], fold_ps[:, D:2 * D]).then_inc(folds_copied, 1)
            dve.wait_ge(folds_done, 2)
            v.tensor_copy(from_x[:, 2 * D:3 * D], fold_ps[:, 2 * D:3 * D])
            v.tensor_copy(from_agg[:, D:2 * D - 1], fold_ps[:, 3 * D:4 * D - 1]
                          ).then_inc(folds_copied, 1)

            for q in range(1, GROUPS, 2):
                dve.wait_ge(x_products, q + 1)
                rows = slice(q * GROUP, (q + 1) * GROUP)
                v.tensor_copy(y[:, rows, 0:D - 1], x_ps[:, 1, :, 0:D - 1])
                v.tensor_copy(g[:, rows, :], x_ps[:, 1, :, D:2 * D])
                v.tensor_copy(z[:, rows, :], x_ps[:, 1, :, 2 * D:3 * D]).then_inc(x_copied[1], 1)
            for reader in x_copied:
                dve.wait_ge(reader, GROUPS // 2)

            deg = stat[:, BT:2 * BT]
            n_one = n_final = 0
            for n, (layer, b, final) in enumerate(turns):
                gb, zb, db = (t[:, b * BT:(b + 1) * BT] for t in (g, z, dinv))
                if layer == 1:
                    n_one += 1
                    dve.wait_ge(halves_turned, 2 * n + 2)
                    v.tensor_tensor(gb, tiles_ps[:, :, 0:D], gb, ALU.add).then_inc(rows_mixed, 1)
                    link(v.tensor_scalar(mask[:], tiles_ps[:, :, 2 * D - 1], 1.0, None, ALU.add))
                    v.tensor_tensor(zb[:, :, 0:D - 1], tiles_ps[:, :, D:2 * D - 1], zb[:, :, 0:D - 1],
                                    ALU.add).then_inc(rows_read, 1)
                    link(v.tensor_scalar(deg, mask[:], TINY, None, ALU.max))
                    link(v.tensor_scalar(mask[:], mask[:], 0.0, None, ALU.is_gt))
                    dve.wait_ge(rows_read, n + 1)
                    link(v.reduce_sum(sums[:], zb[:, :, 0:D - 1], AX_X))
                    link(v.tensor_scalar(zb[:, :, D - 1], sums[:], -1.0, None, ALU.mult))
                    dve.wait_ge(squared, n_one)
                    link(v.reduce_sum(sums[:], squares[:], AX_X))
                    v.tensor_scalar(stat[:, 0:BT], sums[:], 1.0 / D, EPS, ALU.mult, ALU.add
                                    ).then_inc(stat_ready, 1)
                    dve.wait_ge(rooted, n_one + n_final)
                    inverse_root(2 * BT)
                    link(v.tensor_tensor(db, rb[:, BT:2 * BT], mask[:], ALU.mult))
                    link(v.tensor_tensor(gain[:], db, rb[:, 0:BT], ALU.mult))
                    v.tensor_tensor(zb, zb, over_features(gain[:]), ALU.mult).then_inc(z_ready, 1)
                    link(v.tensor_tensor(gb, gb, over_features(rb[:, 0:BT]), ALU.mult))
                    dve.wait_ge(z_ready, n_one)
                    link(v.tensor_tensor(mixed[:], zb, over_features(db), ALU.mult))
                    link(v.tensor_tensor(gb, mixed[:], gb, ALU.add))
                    continue
                for a in range(2):
                    tiles = slice(a * HT, (a + 1) * HT)
                    dve.wait_ge(halves_turned, 2 * n + 1 + a)
                    scaled = v.tensor_tensor(mixed[:, tiles], rows_ps[a],
                                             over_features(db[:, tiles]), ALU.mult)
                    if a == 0:
                        link(scaled)
                    else:
                        scaled.then_inc(rows_read, 1)
                        dve.wait_ge(rows_read, n + 1)
                    if final:
                        v.tensor_tensor(mixed[:, tiles], mixed[:, tiles], gb[:, tiles], ALU.add
                                        ).then_inc(halves_mixed, 1)
                    else:
                        link(v.tensor_tensor(gb[:, tiles], mixed[:, tiles], gb[:, tiles], ALU.add))
                if not final:
                    continue
                n_final += 1
                for a in range(2):
                    tiles = slice(a * HT, (a + 1) * HT)
                    dve.wait_ge(halves_squared, 2 * (n_final - 1) + a + 1)
                    v.reduce_sum(sums[:, tiles], squares[:, tiles], AX_X).then_inc(sums_ready, 1)
                dve.wait_ge(sums_ready, 2 * n_final)
                link(v.tensor_scalar(stat[:, 0:BT], sums[:], 1.0 / D, EPS, ALU.mult, ALU.add))
                dve.wait_ge(rooted, n_one + n_final)
                inverse_root(BT)
                v.tensor_tensor(gb, mixed[:], over_features(rb[:, 0:BT]), ALU.mult
                                ).then_inc(out_ready, 1)
                dve.wait_ge(out_ready, n_final)


def kernel(x, adj, L0_gnn_weight, L1_gnn_W):
    import numpy as np
    import concourse.bacc as bacc
    from concourse.bass_utils import run_bass_kernel_spmd

    N, D = x.shape
    blocks, chunks = N // BLOCK, N // P // CHUNK_TILES
    both_halves = lambda a: np.ascontiguousarray(np.concatenate([a, a], axis=0))

    adj = np.asarray(adj).reshape(blocks, BLOCK, chunks, CHUNK_TILES, P)
    adj_chunks = np.ascontiguousarray(adj.transpose(0, 2, 4, 3, 1)).reshape(
        blocks * chunks, P, CHUNK_TILES, BLOCK)
    xT = np.asarray(x).T
    xT_halves = np.concatenate([xT[:, :N // 2], xT[:, N // 2:]], axis=0)
    w0, w1 = np.asarray(L0_gnn_weight), np.asarray(L1_gnn_W)
    weights = both_halves(np.concatenate([w0.T, w1.T], axis=1))
    expand = np.eye(D, dtype=np.float32)
    expand[:, D - 1] = -1.0
    expand[D - 1, :] = 0.0
    ident = np.eye(D, dtype=np.float32)
    cent = ident - np.float32(1.0 / D)
    consts = both_halves(np.concatenate([cent, expand, expand.T], axis=1))

    arrays = {"adj_chunks": adj_chunks, "xT_halves": np.ascontiguousarray(xT_halves),
              "weights": weights, "consts": consts, "identity": both_halves(ident)}
    nc = bacc.Bacc("TRN2", target_bir_lowering=False, num_devices=1)
    args = [nc.dram_tensor(name, a.shape, F32, kind="ExternalInput").ap()
            for name, a in arrays.items()]
    out = nc.dram_tensor("out", (blocks, P, BLOCK // P, D), F32, kind="ExternalOutput").ap()
    two_layers(nc, *args, out)
    r = run_bass_kernel_spmd(nc, [arrays], core_ids=[0])
    got = r.results[0]["out"].reshape(blocks, P, BLOCK // P, D)
    return np.ascontiguousarray(got.transpose(0, 2, 1, 3)).reshape(N, D)
```
